# Optimizing a Trainium2 kernel written in Bass

```python
import numpy as np
import jax
import jax.numpy as jnp

def _softmax(x, axis=-1):
    return jax.nn.softmax(x, axis=axis)

def _gelu(x):
    return jax.nn.gelu(x, approximate=True)

def _silu(x):
    return jax.nn.silu(x)

def _sigmoid(x):
    return jax.nn.sigmoid(x)

def _layernorm(x, axis=-1, eps=1e-05):
    m = jnp.mean(x, axis=axis, keepdims=True)
    v = jnp.var(x, axis=axis, keepdims=True)
    return (x - m) / jnp.sqrt(v + eps)

def _scatter_add(tgt, idx, src, axis=0):
    return tgt.at[idx].add(src)

def _segment_sum(src, seg, n):
    return jax.ops.segment_sum(src, seg, n)
kernel_name = 'mk_dlrm_tower_d1_rec_r8_e5555d'

def setup_inputs(seed: int=0):
    np.random.seed(seed)
    _w = jnp.asarray

    def _rec_inputs():
        import jax
        import jax.numpy as jnp
        _tk = jax.random.key(seed)
        ids = jnp.stack([jax.random.randint(jax.random.fold_in(_tk, 200 + f), (512,), 0, v, jnp.int32) for f, v in enumerate([1250, 12500, 125000, 1000, 1250, 12500, 1250, 12500, 1000, 1000, 12500, 1000, 12500, 1000, 1250, 1250, 1250, 12500, 1000, 1250, 12500, 1250, 1250, 1250, 12500, 1250])], axis=1)
        tbl_0 = 0.05 * jax.random.normal(jax.random.fold_in(_tk, 500 + 0), (1250, 128), jnp.float32)
        tbl_1 = 0.05 * jax.random.normal(jax.random.fold_in(_tk, 500 + 1), (12500, 128), jnp.float32)
        tbl_2 = 0.05 * jax.random.normal(jax.random.fold_in(_tk, 500 + 2), (125000, 128), jnp.float32)
        tbl_3 = 0.05 * jax.random.normal(jax.random.fold_in(_tk, 500 + 3), (1000, 128), jnp.float32)
        tbl_4 = 0.05 * jax.random.normal(jax.random.fold_in(_tk, 500 + 4), (1250, 128), jnp.float32)
        tbl_5 = 0.05 * jax.random.normal(jax.random.fold_in(_tk, 500 + 5), (12500, 128), jnp.float32)
        tbl_6 = 0.05 * jax.random.normal(jax.random.fold_in(_tk, 500 + 6), (1250, 128), jnp.float32)
        tbl_7 = 0.05 * jax.random.normal(jax.random.fold_in(_tk, 500 + 7), (12500, 128), jnp.float32)
        tbl_8 = 0.05 * jax.random.normal(jax.random.fold_in(_tk, 500 + 8), (1000, 128), jnp.float32)
        tbl_9 = 0.05 * jax.random.normal(jax.random.fold_in(_tk, 500 + 9), (1000, 128), jnp.float32)
        tbl_10 = 0.05 * jax.random.normal(jax.random.fold_in(_tk, 500 + 10), (12500, 128), jnp.float32)
        tbl_11 = 0.05 * jax.random.normal(jax.random.fold_in(_tk, 500 + 11), (1000, 128), jnp.float32)
        tbl_12 = 0.05 * jax.random.normal(jax.random.fold_in(_tk, 500 + 12), (12500, 128), jnp.float32)
        tbl_13 = 0.05 * jax.random.normal(jax.random.fold_in(_tk, 500 + 13), (1000, 128), jnp.float32)
        tbl_14 = 0.05 * jax.random.normal(jax.random.fold_in(_tk, 500 + 14), (1250, 128), jnp.float32)
        tbl_15 = 0.05 * jax.random.normal(jax.random.fold_in(_tk, 500 + 15), (1250, 128), jnp.float32)
        tbl_16 = 0.05 * jax.random.normal(jax.random.fold_in(_tk, 500 + 16), (1250, 128), jnp.float32)
        tbl_17 = 0.05 * jax.random.normal(jax.random.fold_in(_tk, 500 + 17), (12500, 128), jnp.float32)
        tbl_18 = 0.05 * jax.random.normal(jax.random.fold_in(_tk, 500 + 18), (1000, 128), jnp.float32)
        tbl_19 = 0.05 * jax.random.normal(jax.random.fold_in(_tk, 500 + 19), (1250, 128), jnp.float32)
        tbl_20 = 0.05 * jax.random.normal(jax.random.fold_in(_tk, 500 + 20), (12500, 128), jnp.float32)
        tbl_21 = 0.05 * jax.random.normal(jax.random.fold_in(_tk, 500 + 21), (1250, 128), jnp.float32)
        tbl_22 = 0.05 * jax.random.normal(jax.random.fold_in(_tk, 500 + 22), (1250, 128), jnp.float32)
        tbl_23 = 0.05 * jax.random.normal(jax.random.fold_in(_tk, 500 + 23), (1250, 128), jnp.float32)
        tbl_24 = 0.05 * jax.random.normal(jax.random.fold_in(_tk, 500 + 24), (12500, 128), jnp.float32)
        tbl_25 = 0.05 * jax.random.normal(jax.random.fold_in(_tk, 500 + 25), (1250, 128), jnp.float32)
        _rk = jax.random.fold_in(_tk, 7)
        r_dense = -0.000520686 + 1.00062 * jax.random.normal(jax.random.fold_in(_rk, 101), (512, 128), jnp.float32)
        W_top1 = 0.0456912 * jax.random.normal(jax.random.fold_in(_tk, 801), (479, 512), jnp.float32)
        W_top2 = 0.0441942 * jax.random.normal(jax.random.fold_in(_tk, 802), (512, 256), jnp.float32)
        W_top3 = 0.0625 * jax.random.normal(jax.random.fold_in(_tk, 803), (256, 1), jnp.float32)
        b_top1 = jnp.zeros((512,), jnp.float32)
        b_top2 = jnp.zeros((256,), jnp.float32)
        return (r_dense, ids, tbl_0, tbl_1, tbl_2, tbl_3, tbl_4, tbl_5, tbl_6, tbl_7, tbl_8, tbl_9, tbl_10, tbl_11, tbl_12, tbl_13, tbl_14, tbl_15, tbl_16, tbl_17, tbl_18, tbl_19, tbl_20, tbl_21, tbl_22, tbl_23, tbl_24, tbl_25, W_top1, b_top1, W_top2, b_top2, W_top3)
    r_dense, ids, tbl_0, tbl_1, tbl_2, tbl_3, tbl_4, tbl_5, tbl_6, tbl_7, tbl_8, tbl_9, tbl_10, tbl_11, tbl_12, tbl_13, tbl_14, tbl_15, tbl_16, tbl_17, tbl_18, tbl_19, tbl_20, tbl_21, tbl_22, tbl_23, tbl_24, tbl_25, W_top1, b_top1, W_top2, b_top2, W_top3 = _rec_inputs()

    def _L0_rec_setup():
        import jax, jax.numpy as jnp
        import numpy as np
        B, NUM_EMBS, D = (2048, 26, 128)
        key = jax.random.key(seed)
        k1, k2 = jax.random.split(key)
        dense = jax.random.normal(k1, (B, D), dtype=jnp.float32)
        embs = jax.random.normal(k2, (B, NUM_EMBS, D), dtype=jnp.float32)
        return {'dense': dense, 'embs': embs}
    _L0_rec_all = _L0_rec_setup()
    _L0_rec_in = {k: v for k, v in _L0_rec_all.items() if k in ()}
    del _L0_rec_all
    return {'r_dense': r_dense, 'ids': ids, 'tbl_0': tbl_0, 'tbl_1': tbl_1, 'tbl_2': tbl_2, 'tbl_3': tbl_3, 'tbl_4': tbl_4, 'tbl_5': tbl_5, 'tbl_6': tbl_6, 'tbl_7': tbl_7, 'tbl_8': tbl_8, 'tbl_9': tbl_9, 'tbl_10': tbl_10, 'tbl_11': tbl_11, 'tbl_12': tbl_12, 'tbl_13': tbl_13, 'tbl_14': tbl_14, 'tbl_15': tbl_15, 'tbl_16': tbl_16, 'tbl_17': tbl_17, 'tbl_18': tbl_18, 'tbl_19': tbl_19, 'tbl_20': tbl_20, 'tbl_21': tbl_21, 'tbl_22': tbl_22, 'tbl_23': tbl_23, 'tbl_24': tbl_24, 'tbl_25': tbl_25, 'W_top1': W_top1, 'b_top1': b_top1, 'W_top2': W_top2, 'b_top2': b_top2, 'W_top3': W_top3}

def reference(r_dense, ids, tbl_0, tbl_1, tbl_2, tbl_3, tbl_4, tbl_5, tbl_6, tbl_7, tbl_8, tbl_9, tbl_10, tbl_11, tbl_12, tbl_13, tbl_14, tbl_15, tbl_16, tbl_17, tbl_18, tbl_19, tbl_20, tbl_21, tbl_22, tbl_23, tbl_24, tbl_25, W_top1, b_top1, W_top2, b_top2, W_top3):
    import jax
    import jax.numpy as jnp

    def _L0_rec_ref(dense, embs):
        import jax, jax.numpy as jnp
        import numpy as np
        B, NUM_EMBS, D = (2048, 26, 128)
        T = jnp.concatenate([dense[:, None, :], embs], axis=1)
        N = T.shape[1]
        Z = jnp.einsum('bnd,bmd->bnm', T, T)
        iu0, iu1 = jnp.triu_indices(N, k=1)
        return Z[:, iu0, iu1]
    e = jnp.stack([tbl_0[ids[:, 0]], tbl_1[ids[:, 1]], tbl_2[ids[:, 2]], tbl_3[ids[:, 3]], tbl_4[ids[:, 4]], tbl_5[ids[:, 5]], tbl_6[ids[:, 6]], tbl_7[ids[:, 7]], tbl_8[ids[:, 8]], tbl_9[ids[:, 9]], tbl_10[ids[:, 10]], tbl_11[ids[:, 11]], tbl_12[ids[:, 12]], tbl_13[ids[:, 13]], tbl_14[ids[:, 14]], tbl_15[ids[:, 15]], tbl_16[ids[:, 16]], tbl_17[ids[:, 17]], tbl_18[ids[:, 18]], tbl_19[ids[:, 19]], tbl_20[ids[:, 20]], tbl_21[ids[:, 21]], tbl_22[ids[:, 22]], tbl_23[ids[:, 23]], tbl_24[ids[:, 24]], tbl_25[ids[:, 25]]], axis=1)
    z = _L0_rec_ref(r_dense, e)
    z = z.reshape(z.shape[0], -1)
    h = jnp.concatenate([z, r_dense], axis=1)
    h = jnp.maximum(h @ W_top1 + b_top1, 0.0)
    h = jnp.maximum(h @ W_top2 + b_top2, 0.0)
    y = h @ W_top3
    return y

_drawn_inputs = setup_inputs


def setup_inputs(seed=0):
    import zlib

    import numpy as np

    out = dict(_drawn_inputs(seed))
    spreads = {'b_top1': (0.0, 0.1), 'b_top2': (0.0, 0.1)}
    factors = {}
    for name, (base, spread) in spreads.items():
        noise = np.random.default_rng([zlib.crc32(name.encode()), seed]).standard_normal(out[name].shape)
        drawn = base * np.exp(spread * noise) if base else spread * noise
        out[name] = jnp.asarray(drawn.astype(out[name].dtype))
    for name, factor in factors.items():
        out[name] = (out[name] * factor).astype(out[name].dtype)
    return out
```

```python
import numpy as np

import concourse.bass as bass
from concourse import mybir
from contextlib import ExitStack

P = 128
B = 512
D = 128
TILES = B // P
ROWS = [1250, 12500, 125000, 1000, 1250, 12500, 1250, 12500, 1000, 1000, 12500, 1000, 12500,
        1000, 1250, 1250, 1250, 12500, 1000, 1250, 12500, 1250, 1250, 1250, 12500, 1250]
TABLES = len(ROWS)
FEATURES = TABLES + 1
HIDDEN1, HIDDEN2 = 512, 256
N1, N2 = HIDDEN1 // P, HIDDEN2 // P

SELECT_PARTS = 125
SELECTED_COUNT = 10
SELECTED = sorted((f for f in range(TABLES) if ROWS[f] <= 1250), key=lambda f: ROWS[f])[:SELECTED_COUNT]
GATHERED = [f for f in range(TABLES) if f not in SELECTED]
GROUP = 4
GROUPS = len(GATHERED) // GROUP
assert len(GATHERED) % GROUP == 0

SLOTS = 32
SLOT_FEATURE = [f + 1 for f in GATHERED] + [f + 1 for f in SELECTED] + [0]
DENSE_SLOT = FEATURES - 1
SELECT_SLOT0 = len(GATHERED)

MOVING = FEATURES - 1
SAMPLES_PER_PRODUCT = P // SLOTS
PRODUCT_COLS = SAMPLES_PER_PRODUCT * MOVING
PRODUCTS_PER_BANK = 4
BATCH_BANKS = 2
BATCH_SAMPLES = BATCH_BANKS * PRODUCTS_PER_BANK * SAMPLES_PER_PRODUCT
BATCHES = P // BATCH_SAMPLES
QUADS = P // SLOTS
PAIR_CHUNKS = -(-MOVING // QUADS)
DENSE_CHUNK = PAIR_CHUNKS
CHUNKS1 = PAIR_CHUNKS + 1

RING = 12
TABLE_BUFFERS = 3
MLP_GROUPS = [(0, 2), (2, 3), (3, 4)]


def quads_in(chunk):
    return min(QUADS, MOVING - QUADS * chunk)


def build(nc, idx, ids_by_table, dense_t, tables, w1, w2, columns, out):
    fp32, i32 = mybir.dt.float32, mybir.dt.int32
    ALU, ACT = mybir.AluOpType, mybir.ActivationFunctionType

    with ExitStack() as ctx:
        def sb(name, shape, dt=fp32):
            return ctx.enter_context(nc.sbuf_tensor(name, shape, dt))

        def sem(name):
            return ctx.enter_context(nc.semaphore(name))

        idx_sb = sb("idx_sb", [P, TILES, TABLES], i32)
        ids_all = sb("ids_all", [P, SELECTED_COUNT, B], i32)
        row_no = sb("row_no", [P, 18])
        identity = sb("identity", [P, P])
        table_sb = sb("table_sb", [P, TABLE_BUFFERS, 10, D])
        onehot = sb("onehot", [P, RING, B])
        rows = sb("rows", [P, TILES, len(GATHERED), D])
        featT = sb("featT", [P, TILES, P, SLOTS])
        denseT = sb("denseT", [P, B])
        pairs = sb("pairs", [P, PAIR_CHUNKS, B])
        w1_sb = sb("w1_sb", [P, CHUNKS1, HIDDEN1])
        w2_sb = sb("w2_sb", [P, N1, HIDDEN2])
        cols_sb = sb("cols_sb", [P, N1 + N2 + N2])
        h1T = sb("h1T", [P, N1, B])
        h2T = sb("h2T", [P, N2, B])
        y = sb("y", [1, B])

        work = ctx.enter_context(nc.psum_tensor("work", [P, 2, 512], fp32))
        rowsT = ctx.enter_context(nc.psum_tensor("rowsT", [P, 2, GROUP, P], fp32))
        gram = ctx.enter_context(nc.psum_tensor("gram", [P, 2 * BATCH_BANKS, 512], fp32))

        b1 = cols_sb[:, 0:N1]
        b2 = cols_sb[:, N1:N1 + N2]
        w3 = cols_sb[:, N1 + N2:N1 + 2 * N2]
        row_no_at = {8: 0, 10: 8}

        idx_landed = sem("idx_landed")
        ids_landed = [sem(f"ids_landed{k}") for k in range(3)]
        table_landed = [sem(f"table_landed{k}") for k in range(TABLE_BUFFERS)]
        dense_landed = sem("dense_landed")
        w1_landed = sem("w1_landed")
        w2_landed = sem("w2_landed")
        cols_landed = sem("cols_landed")
        rows_landed = [sem(f"rows_landed{s}") for s in range(len(GATHERED))]
        identity_zeroed = sem("identity_zeroed")
        identity_ready = sem("identity_ready")
        row_no_ready = sem("row_no_ready")
        padding_zeroed = sem("padding_zeroed")
        dense_copied = sem("dense_copied")
        onehot_built = sem("onehot_built")
        chunk_selected = sem("chunk_selected")
        selected_copied = sem("selected_copied")
        transposed = sem("transposed")
        rowsT_copied = sem("rowsT_copied")
        products = sem("products")
        pairs_by_dve = sem("pairs_by_dve")
        pairs_by_act = sem("pairs_by_act")
        h1_summed = sem("h1_summed")
        h1_done = sem("h1_done")
        h2_summed = sem("h2_summed")
        h2_done = sem("h2_done")
        y_summed = sem("y_summed")
        y_done = sem("y_done")
        stored = sem("stored")

        ids_parts = [(0, 1), (1, 4), (4, SELECTED_COUNT)]
        ids_part = [next(n for n, (a, b) in enumerate(ids_parts) if a <= k < b) for k in range(SELECTED_COUNT)]
        places = [ROWS[f] // SELECT_PARTS for f in SELECTED]
        chunk0 = [sum(places[:k]) for k in range(SELECTED_COUNT + 1)]

        block = ctx.enter_context(nc.Block())

        @block.sync
        def _(sp):
            sp.dma_start(idx_sb[:], idx.rearrange("p (t f) -> p t f", t=TILES)).then_inc(idx_landed, 16)
            for k in range(SELECTED_COUNT):
                part = ids_part[k]
                lo, hi = ids_parts[part]
                if k == lo:
                    sp.dma_start(ids_all[:, lo:hi, :], ids_by_table[lo:hi, :].unsqueeze(0).broadcast_to([P, hi - lo, B])
                                 ).then_inc(ids_landed[part], 16)
                buf, n = k % TABLE_BUFFERS, places[k]
                if k >= TABLE_BUFFERS:
                    sp.wait_ge(chunk_selected, chunk0[k - TABLE_BUFFERS + 1])
                src = tables[SELECTED[k]].rearrange("(p r) d -> p (r d)", r=n)
                dst = table_sb[:, buf, 0:n, :].rearrange("p r d -> p (r d)")
                for lo_p, hi_p in ((0, 112), (112, SELECT_PARTS)):
                    sp.dma_start(dst[lo_p:hi_p], src[lo_p:hi_p]).then_inc(table_landed[buf], 16)
                if k == 1:
                    sp.dma_start(denseT[:], dense_t).then_inc(dense_landed, 16)
                if k == 5:
                    sp.dma_start(w1_sb[:], w1.rearrange("p (c n) -> p c n", c=CHUNKS1)).then_inc(w1_landed, 16)
                    sp.dma_start(w2_sb[:], w2.rearrange("p (c n) -> p c n", c=N1)).then_inc(w2_landed, 16)
                    sp.dma_start(cols_sb[:], columns).then_inc(cols_landed, 16)
            sp.wait_ge(y_done, len(MLP_GROUPS))
            sp.dma_start(out.rearrange("b o -> o b"), y[:]).then_inc(stored, 16)
            sp.wait_ge(stored, 16)

        @block.gpsimd
        def _(pool):
            for n, at in row_no_at.items():
                nc.gpsimd.iota(row_no[:, at:at + n], pattern=[[1, n]], base=0, channel_multiplier=n,
                               allow_small_or_imprecise_dtypes=True).then_inc(row_no_ready, 1)
            nc.gpsimd.memset(identity[:], 0.0).then_inc(identity_zeroed, 1)
            pool.wait_ge(identity_zeroed, 1)
            nc.gpsimd.affine_select(out=identity[:], in_=identity[:], compare_op=ALU.not_equal, fill=1.0, base=0,
                                    pattern=[[-1, P]], channel_multiplier=1).then_inc(identity_ready, 1)
            pool.wait_ge(idx_landed, 16)
            for t in range(TILES):
                for s, f in enumerate(GATHERED):
                    if t >= 1:
                        pool.wait_ge(rows_landed[s], 16 * t)
                    pool.indirect_dma_start(
                        rows[:, t, s, :], None, tables[f],
                        bass.IndirectOffsetOnAxis(ap=idx_sb[:, t, f:f + 1], axis=0)).then_inc(rows_landed[s], 16)

        def batch_view(n, b4):
            half = n % 2
            v = gram[SLOTS * b4:SLOTS * (b4 + 1), BATCH_BANKS * half:BATCH_BANKS * (half + 1),
                     0:PRODUCTS_PER_BANK * PRODUCT_COLS]
            return v.rearrange("p k (g b j) -> p k g b j", g=PRODUCTS_PER_BANK, b=SAMPLES_PER_PRODUCT)[:, :, :, b4, :]

        def pairs_view(n, b4, q, chunks):
            v = pairs[SLOTS * q:SLOTS * (q + 1), 0:chunks, BATCH_SAMPLES * n:BATCH_SAMPLES * (n + 1)]
            return v.rearrange("p c (k g b) -> p c k g b", k=BATCH_BANKS, b=SAMPLES_PER_PRODUCT)[:, :, :, :, b4]

        def pair_copies(copy, n, samples):
            for b4 in samples:
                for q in range(QUADS):
                    chunks = PAIR_CHUNKS if q < quads_in(PAIR_CHUNKS - 1) else PAIR_CHUNKS - 1
                    src = batch_view(n, b4)[:, :, :, q:MOVING:QUADS].rearrange("p k g c -> p c k g")
                    last = copy(pairs_view(n, b4, q, chunks), src)
            return last

        def copy_group(act, m):
            t, g = m // GROUPS, m % GROUPS
            act.wait_ge(transposed, m + 1)
            dst = featT[:, t, :, GROUP * g:GROUP * (g + 1)].rearrange("p b f -> p f b")
            nc.scalar.copy(dst, rowsT[:, m % 2]).then_inc(rowsT_copied, 1)

        PHASE1_GROUPS = 2 * GROUPS

        @block.scalar
        def _(act):
            for k in range(SELECTED_COUNT):
                act.wait_ge(chunk_selected, chunk0[k + 1])
                dst = featT[:, :, :, SELECT_SLOT0 + k].rearrange("p t b -> p (t b)")
                nc.scalar.copy(dst, work[:, k % 2, :]).then_inc(selected_copied, 1)
                if k < PHASE1_GROUPS:
                    copy_group(act, k)

            def batches(t):
                for n in range(BATCHES * t, BATCHES * (t + 1)):
                    act.wait_ge(products, n + 1)
                    pair_copies(nc.scalar.copy, n, (2, 3)).then_inc(pairs_by_act, 1)

            def mlp(m):
                lo, hi = (P * t for t in MLP_GROUPS[m])
                if m == 0:
                    act.wait_ge(cols_landed, 16)
                for u in range(N1):
                    act.wait_ge(h1_summed, N1 * m + u + 1)
                    nc.scalar.activation(h1T[:, u, lo:hi], work[:, u % 2, 0:hi - lo], ACT.Relu,
                                         bias=b1[:, u:u + 1]).then_inc(h1_done, 1)
                for u in range(N2):
                    act.wait_ge(h2_summed, N2 * m + u + 1)
                    nc.scalar.activation(h2T[:, u, lo:hi], work[:, u % 2, 0:hi - lo], ACT.Relu,
                                         bias=b2[:, u:u + 1]).then_inc(h2_done, 1)
                act.wait_ge(y_summed, m + 1)
                nc.scalar.copy(y[0:1, lo:hi], work[0:1, 0, 0:hi - lo]).then_inc(y_done, 1)

            batches(0)
            copy_group(act, 2 * GROUPS)
            batches(1)
            copy_group(act, 2 * GROUPS + 1)
            mlp(0)
            copy_group(act, 2 * GROUPS + 2)
            copy_group(act, 2 * GROUPS + 3)
            batches(2)
            copy_group(act, 3 * GROUPS)
            copy_group(act, 3 * GROUPS + 1)
            mlp(1)
            copy_group(act, 3 * GROUPS + 2)
            copy_group(act, 3 * GROUPS + 3)
            batches(3)
            mlp(2)

        @block.vector
        def _(dve):
            nc.vector.memset(featT[:, :, :, FEATURES:SLOTS], 0.0).then_inc(padding_zeroed, 1)
            dve.wait_ge(row_no_ready, len(row_no_at))
            for k in range(SELECTED_COUNT):
                if k == ids_parts[ids_part[k]][0]:
                    dve.wait_ge(ids_landed[ids_part[k]], 16)
                for c in range(places[k]):
                    n = chunk0[k] + c
                    if n >= RING:
                        dve.wait_ge(chunk_selected, n - RING + 1)
                    at = row_no_at[places[k]] + c
                    nc.vector.tensor_scalar(onehot[0:SELECT_PARTS, n % RING, :], ids_all[0:SELECT_PARTS, k, :],
                                            row_no[0:SELECT_PARTS, at:at + 1], None,
                                            ALU.is_equal).then_inc(onehot_built, 1)
                if k == 1:
                    dve.wait_ge(dense_landed, 16)
                    nc.vector.tensor_copy(featT[:, :, :, DENSE_SLOT].rearrange("p t b -> p (t b)"),
                                          denseT[:]).then_inc(dense_copied, 1)
            for n in range(TILES * BATCHES):
                dve.wait_ge(products, n + 1)
                pair_copies(nc.vector.tensor_copy, n, (0, 1)).then_inc(pairs_by_dve, 1)

        @block.tensor
        def _(pe):
            def select(k):
                buf = k % TABLE_BUFFERS
                pe.wait_ge(table_landed[buf], 32 * (k // TABLE_BUFFERS + 1))
                if k >= 2:
                    pe.wait_ge(selected_copied, k - 1)
                for c in range(places[k]):
                    n = chunk0[k] + c
                    pe.wait_ge(onehot_built, n + 1)
                    nc.tensor.matmul(work[:, k % 2, :], table_sb[0:SELECT_PARTS, buf, c, :],
                                     onehot[0:SELECT_PARTS, n % RING, :],
                                     start=(c == 0), stop=(c == places[k] - 1)).then_inc(chunk_selected, 1)

            def transpose_group(m):
                t, g = m // GROUPS, m % GROUPS
                if m == 0:
                    pe.wait_ge(identity_ready, 1)
                if m >= 2:
                    pe.wait_ge(rowsT_copied, m - 1)
                for i in range(GROUP):
                    s = GROUP * g + i
                    pe.wait_ge(rows_landed[s], 16 * (t + 1))
                    last = nc.tensor.transpose(rowsT[:, m % 2, i, :], rows[:, t, s, :], identity[:])
                last.then_inc(transposed, 1)

            def batch(n):
                if n % BATCHES == 0:
                    pe.wait_ge(rowsT_copied, GROUPS * (n // BATCHES + 1))
                if n >= 2:
                    pe.wait_ge(pairs_by_dve, n - 1)
                    pe.wait_ge(pairs_by_act, n - 1)
                t = n // BATCHES
                for m in range(BATCH_BANKS * PRODUCTS_PER_BANK):
                    b = BATCH_SAMPLES * (n % BATCHES) + SAMPLES_PER_PRODUCT * m
                    four = featT[:, t, b:b + SAMPLES_PER_PRODUCT, :]
                    col = PRODUCT_COLS * (m % PRODUCTS_PER_BANK)
                    dst = gram[:, BATCH_BANKS * (n % 2) + m // PRODUCTS_PER_BANK, col:col + PRODUCT_COLS]
                    last = nc.tensor.matmul(dst, four.rearrange("p b s -> p (b s)"), four[:, :, 1:FEATURES],
                                            start=True, stop=True)
                last.then_inc(products, 1)

            def layer1(m, u):
                lo, hi = (P * t for t in MLP_GROUPS[m])
                if u >= 2:
                    pe.wait_ge(h1_done, N1 * m + u - 1)
                elif m >= 1:
                    pe.wait_ge(y_done, m)
                dst = work[:, u % 2, 0:hi - lo]
                cols = slice(P * u, P * (u + 1))
                nc.tensor.matmul(dst, w1_sb[:, DENSE_CHUNK, cols], denseT[:, lo:hi], start=True, stop=False)
                if u == 0:
                    pe.wait_ge(pairs_by_dve, BATCHES * MLP_GROUPS[m][1])
                    pe.wait_ge(pairs_by_act, BATCHES * MLP_GROUPS[m][1])
                for c in range(PAIR_CHUNKS):
                    k = SLOTS * quads_in(c)
                    last = nc.tensor.matmul(dst, w1_sb[0:k, c, cols], pairs[0:k, c, lo:hi],
                                            start=False, stop=(c == PAIR_CHUNKS - 1))
                last.then_inc(h1_summed, 1)

            def layers2_3(m):
                lo, hi = (P * t for t in MLP_GROUPS[m])
                for u in range(N2):
                    for c in range(N1):
                        pe.wait_ge(h1_done, N1 * m + max(c + 1, N1 - 1 + u))
                        last = nc.tensor.matmul(work[:, u % 2, 0:hi - lo], w2_sb[:, c, P * u:P * (u + 1)],
                                                h1T[:, c, lo:hi], start=(c == 0), stop=(c == N1 - 1))
                    last.then_inc(h2_summed, 1)
                for c in range(N2):
                    pe.wait_ge(h2_done, N2 * m + c + 1)
                    last = nc.tensor.matmul(work[0:1, 0, 0:hi - lo], w3[:, c:c + 1], h2T[:, c, lo:hi],
                                            start=(c == 0), stop=(c == N2 - 1))
                last.then_inc(y_summed, 1)

            def mlp(m):
                for u in range(N1):
                    layer1(m, u)
                layers2_3(m)

            def batches(t):
                for n in range(BATCHES * t, BATCHES * (t + 1)):
                    batch(n)

            for k in range(SELECTED_COUNT):
                select(k)
                if k < PHASE1_GROUPS:
                    transpose_group(k)
            pe.wait_ge(selected_copied, SELECTED_COUNT)
            pe.wait_ge(dense_copied, 1)
            pe.wait_ge(padding_zeroed, 1)
            batches(0)
            transpose_group(2 * GROUPS)
            batches(1)
            transpose_group(2 * GROUPS + 1)
            pe.wait_ge(w1_landed, 16)
            pe.wait_ge(w2_landed, 16)
            pe.wait_ge(cols_landed, 16)
            mlp(0)
            transpose_group(2 * GROUPS + 2)
            transpose_group(2 * GROUPS + 3)
            batches(2)
            transpose_group(3 * GROUPS)
            transpose_group(3 * GROUPS + 1)
            mlp(1)
            transpose_group(3 * GROUPS + 2)
            transpose_group(3 * GROUPS + 3)
            batches(3)
            mlp(2)


def pair_row(a, b):
    return a * (FEATURES - 1) - a * (a - 1) // 2 + (b - a - 1)


def arrange_w1(w):
    arranged = np.zeros((P, CHUNKS1, HIDDEN1), w.dtype)
    for j in range(1, FEATURES):
        c, q = divmod(j - 1, QUADS)
        for i in range(j):
            a, b = sorted((SLOT_FEATURE[i], SLOT_FEATURE[j]))
            arranged[SLOTS * q + i, c] = w[pair_row(a, b)]
    arranged[:, DENSE_CHUNK] = w[FEATURES * (FEATURES - 1) // 2:]
    return arranged.reshape(P, CHUNKS1 * HIDDEN1)


def by_column(v):
    return v.reshape(-1, P).T


def kernel(**inputs):
    import concourse.bacc as bacc
    from concourse.bass_utils import run_bass_kernel_spmd

    ids, dense = np.asarray(inputs["ids"]), np.asarray(inputs["r_dense"])
    w2 = np.asarray(inputs["W_top2"])
    host = {
        "idx": ids.reshape(TILES, P, TABLES).transpose(1, 0, 2).reshape(P, TILES * TABLES),
        "ids_by_table": ids.T[SELECTED],
        "dense_t": dense.T,
        **{f"tbl_{f}": np.asarray(inputs[f"tbl_{f}"]) for f in range(TABLES)},
        "w1": arrange_w1(np.asarray(inputs["W_top1"])),
        "w2": w2.reshape(N1, P, HIDDEN2).transpose(1, 0, 2).reshape(P, N1 * HIDDEN2),
        "columns": np.concatenate([by_column(np.asarray(inputs["b_top1"])), by_column(np.asarray(inputs["b_top2"])),
                                   by_column(np.asarray(inputs["W_top3"]))], axis=1),
    }
    host = {name: np.ascontiguousarray(a) for name, a in host.items()}
    nc = bacc.Bacc("TRN2", target_bir_lowering=False, num_devices=1)
    aps = {name: nc.dram_tensor(name, a.shape, mybir.dt.from_np(a.dtype), kind="ExternalInput").ap()
           for name, a in host.items()}
    out = nc.dram_tensor("y_out", (B, 1), mybir.dt.float32, kind="ExternalOutput").ap()
    build(nc, aps["idx"], aps["ids_by_table"], aps["dense_t"], [aps[f"tbl_{f}"] for f in range(TABLES)],
          aps["w1"], aps["w2"], aps["columns"], out)
    return run_bass_kernel_spmd(nc, [host], core_ids=[0]).results[0]["y_out"]
```

```python
import numpy as np

import concourse.bass as bass
from concourse import mybir
from contextlib import ExitStack

P = 128
B = 512
D = 128
TILES = B // P
ROWS = [1250, 12500, 125000, 1000, 1250, 12500, 1250, 12500, 1000, 1000, 12500, 1000, 12500,
        1000, 1250, 1250, 1250, 12500, 1000, 1250, 12500, 1250, 1250, 1250, 12500, 1250]
TABLES = len(ROWS)
FEATURES = TABLES + 1
HIDDEN1, HIDDEN2 = 512, 256
N1 = HIDDEN1 // P

SELECT_PARTS = 125
SELECTED_COUNT = 8
SELECTED = sorted((f for f in range(TABLES) if ROWS[f] <= 1250), key=lambda f: ROWS[f])[:SELECTED_COUNT]
GATHERED = [f for f in range(TABLES) if f not in SELECTED]
PLACES = [ROWS[f] // SELECT_PARTS for f in SELECTED]
MAX_PLACES = max(PLACES)
CHUNK0 = [sum(PLACES[:k]) for k in range(SELECTED_COUNT + 1)]
ROW0_AT = {n: at for at, n in enumerate(sorted(set(PLACES)))}
GROUP = 4
GROUPS = -(-len(GATHERED) // GROUP)

SLOTS = 32
SLOT_FEATURE = [f + 1 for f in GATHERED] + [f + 1 for f in SELECTED] + [0]
DENSE_SLOT = FEATURES - 1
SELECT_SLOT0 = len(GATHERED)

MOVING = FEATURES - 1
FOUR = P // SLOTS
PRODUCT_COLS = FOUR * MOVING
PRODUCTS_PER_BANK = 4
BATCH_BANKS = 2
BATCH_PRODUCTS = BATCH_BANKS * PRODUCTS_PER_BANK
BATCHES = P // (BATCH_PRODUCTS * FOUR)

HALF = SLOTS // 2
WIDE = MOVING - HALF + 1
NARROW = HALF - 1
TAIL_COLUMNS = HALF - WIDE
BIAS_AT = WIDE * SLOTS
PACKED = 3 * P
assert BIAS_AT < PACKED and TAIL_COLUMNS * (TAIL_COLUMNS + 1) // 2 <= HALF


def packed_at(j):
    if j >= HALF:
        return SLOTS * (j - HALF)
    if j > TAIL_COLUMNS:
        w = HALF - j
        return SLOTS * w + HALF + w
    return HALF + j * (j - 1) // 2


PAIR_CHUNKS = PACKED // P
DENSE_CHUNK = PAIR_CHUNKS
CHUNKS1 = PAIR_CHUNKS + 1

ONEHOTS = 12
IDS_BUFFERS = 3
PART_BUFFERS = 3
AHEAD = 2
RAW_BUFFERS = 3
WEIGHT_LOADS = 3
WEIGHT_COLS = CHUNKS1 * HIDDEN1 // 2
LOADS = SELECTED_COUNT + WEIGHT_LOADS


def raw_landed_at(n):
    return sum(32 if m < SELECTED_COUNT else 16 for m in range(n % RAW_BUFFERS, n + 1, RAW_BUFFERS))


def schedule():
    groups = iter(range(GROUPS * TILES))

    def rows(count=1):
        for _ in range(count):
            yield "rows", next(groups)

    mlp = lambda t: ([("dense", t), ("pairsT", t)], [("layer1", t)], [("hiddenT", t)], [("layer2", t)])

    for k in range(SELECTED_COUNT):
        yield "select", k
        if k == 1:
            yield "dense_in", 0
        yield from rows()
    for n in range(BATCHES):
        yield "products", n
        if n < WEIGHT_LOADS:
            yield "weights_in", n
        if n < 2 * GROUPS - SELECTED_COUNT:
            yield from rows()
    yield "pack", 0
    for t in range(1, TILES):
        for n, step in enumerate(mlp(t - 1)):
            if t + 1 < TILES and n == 0:
                yield from rows(GROUPS - BATCHES)
            yield "products", BATCHES * t + n
            if n == BATCHES - 1:
                yield "pack", t
            yield from step
            if t + 1 < TILES:
                yield from rows()
    for step in mlp(TILES - 1):
        yield from step


SCHEDULE = list(schedule())


def build(nc, idx, ids_by_table, dense_t, tables, w1, w2, b2, w3, out):
    fp32, fp32r, i32 = mybir.dt.float32, mybir.dt.float32r, mybir.dt.int32
    ALU, ACT = mybir.AluOpType, mybir.ActivationFunctionType

    with ExitStack() as ctx:
        def sb(name, shape, dt=fp32):
            return ctx.enter_context(nc.sbuf_tensor(name, shape, dt))

        def sem(name):
            return ctx.enter_context(nc.semaphore(name))

        idx_sb = sb("idx_sb", [P, TILES, TABLES], i32)
        ids_all = sb("ids_all", [P, IDS_BUFFERS, B], i32)
        ids_rel = sb("ids_rel", [P, IDS_BUFFERS, B])
        minus_row0 = sb("minus_row0", [P, len(ROW0_AT)])
        partition = sb("partition", [P, 1])
        identity = sb("identity", [P, P])
        raw = sb("raw", [P, RAW_BUFFERS, MAX_PLACES * D])
        table_h = sb("table_h", [P, PART_BUFFERS, MAX_PLACES, D], fp32r)
        table_l = sb("table_l", [P, PART_BUFFERS, MAX_PLACES, D], fp32r)
        onehot = sb("onehot", [P, ONEHOTS, B], fp32r)
        rows = sb("rows", [P, 2, len(GATHERED), D])
        featT = sb("featT", [P, TILES, P // FOUR, FOUR, SLOTS])
        denseT = sb("denseT", [P, B])
        dense_h = sb("dense_h", [P, B], fp32r)
        dense_l = sb("dense_l", [P, B], fp32r)
        diag = sb("diag", [P, 2, MOVING, SLOTS])
        narrow = sb("narrow", [P, NARROW, SLOTS])
        packed = sb("packed", [P, 2, PACKED])
        pairs_h = sb("pairs_h", [P, PAIR_CHUNKS, P], fp32r)
        pairs_l = sb("pairs_l", [P, PAIR_CHUNKS, P], fp32r)
        w1_h, w1_l = onehot[:, 0:CHUNKS1, :], onehot[:, CHUNKS1:2 * CHUNKS1, :]
        w2_h, w2_l = (onehot[:, at:at + N1 // 2, :].rearrange("p c (u n) -> p (c u) n", n=HIDDEN2)
                      for at in (2 * CHUNKS1, 2 * CHUNKS1 + N1 // 2))
        b2_all = sb("b2_all", [P, HIDDEN2])
        w3_all = sb("w3_all", [P, HIDDEN2])
        h1 = sb("h1", [P, N1, P])
        h1T_h = sb("h1T_h", [P, N1, P], fp32r)
        h1T_l = sb("h1T_l", [P, N1, P], fp32r)
        h2 = sb("h2", [P, HIDDEN2])
        h2_w3 = sb("h2_w3", [P, HIDDEN2])
        y = sb("y", [P, TILES])

        sums = ctx.enter_context(nc.psum_tensor("sums", [P, 2, 512], fp32))
        rowsT = ctx.enter_context(nc.psum_tensor("rowsT", [P, GROUP, P], fp32))
        mlpT = ctx.enter_context(nc.psum_tensor("mlpT", [P, N1, P], fp32))
        gram = ctx.enter_context(nc.psum_tensor("gram", [P, 2 * BATCH_BANKS, 512], fp32))

        idx_landed = sem("idx_landed")
        ids_landed = [sem(f"ids_landed{k}") for k in range(IDS_BUFFERS)]
        raw_landed = [sem(f"raw_landed{k}") for k in range(RAW_BUFFERS)]
        dense_landed = sem("dense_landed")
        b2_landed = sem("b2_landed")
        w3_landed = sem("w3_landed")
        rows_landed = [sem(f"rows_landed{s}") for s in range(len(GATHERED))]
        identity_zeroed = sem("identity_zeroed")
        identity_ready = sem("identity_ready")
        partition_ready = sem("partition_ready")
        row0_ready = sem("row0_ready")
        ids_rel_done = sem("ids_rel_done")
        padding_set = sem("padding_set")
        packed_set = sem("packed_set")
        load_high = sem("load_high")
        load_low = sem("load_low")
        dense_copied = sem("dense_copied")
        dense_high = sem("dense_high")
        dense_low = sem("dense_low")
        onehot_built = sem("onehot_built")
        chunk_selected = sem("chunk_selected")
        selected_copied = sem("selected_copied")
        rows_turned = sem("rows_turned")
        rows_copied = sem("rows_copied")
        products_done = sem("products_done")
        diag_by_dve = sem("diag_by_dve")
        diag_by_act = sem("diag_by_act")
        wide_turned = sem("wide_turned")
        narrow_turned = sem("narrow_turned")
        packed_by_dve = sem("packed_by_dve")
        packed_by_act = sem("packed_by_act")
        pairs_turned = sem("pairs_turned")
        pairs_high = sem("pairs_high")
        pairs_low = sem("pairs_low")
        h1_summed = sem("h1_summed")
        h1_done = sem("h1_done")
        h1_turned = sem("h1_turned")
        h1_high = sem("h1_high")
        h1_low = sem("h1_low")
        h2_summed = sem("h2_summed")
        h2_biased = sem("h2_biased")
        y_done = sem("y_done")
        stored = [sem(f"stored{t}") for t in range(TILES)]

        def slot_view(slot):
            return featT[:, :, :, :, slot].rearrange("p t g b -> p t b g")

        def by_sample(x):
            return x.rearrange("p (t b g) -> p t b g", t=TILES, b=FOUR)

        def group_slots(m):
            return range(GROUP * (m % GROUPS), min(GROUP * (m % GROUPS) + GROUP, len(GATHERED)))

        def high_low(n):
            if n < SELECTED_COUNT:
                cols = PLACES[n] * D
                return [x[0:SELECT_PARTS, n % PART_BUFFERS, 0:PLACES[n], :].rearrange("p r d -> p (r d)")
                        for x in (table_h, table_l)] + [SELECT_PARTS, cols]
            n -= SELECTED_COUNT
            if n < 2:
                half = CHUNKS1 // 2
                return [x[:, half * n:half * (n + 1), :].rearrange("p c n -> p (c n)")
                        for x in (w1_h, w1_l)] + [P, WEIGHT_COLS]
            return [x.rearrange("p c n -> p (c n)") for x in (w2_h, w2_l)] + [P, N1 * HIDDEN2]

        def table_parts(n):
            cols = PLACES[n] * D
            src = tables[SELECTED[n]].rearrange("(p r) d -> p (r d)", r=PLACES[n])
            return [(raw[lo:hi, n % RAW_BUFFERS, 0:cols], src[lo:hi]) for lo, hi in ((0, 112), (112, SELECT_PARTS))]

        block = ctx.enter_context(nc.Block())

        @block.sync
        def _(sp):
            sp.dma_start(idx_sb[:], idx.rearrange("p (t f) -> p t f", t=TILES)).then_inc(idx_landed, 16)
            for n in range(LOADS):
                buf = n % RAW_BUFFERS
                if n < SELECTED_COUNT:
                    if n >= IDS_BUFFERS:
                        sp.wait_ge(ids_rel_done, n - IDS_BUFFERS + 1)
                    sp.dma_start(ids_all[:, n % IDS_BUFFERS, :], ids_by_table[n:n + 1, :].broadcast_to([P, B])
                                 ).then_inc(ids_landed[n % IDS_BUFFERS], 16)
                if n == 0:
                    continue
                if n >= RAW_BUFFERS:
                    sp.wait_ge(load_low, n - RAW_BUFFERS + 1)
                if n < SELECTED_COUNT:
                    for dst, src in table_parts(n):
                        sp.dma_start(dst, src).then_inc(raw_landed[buf], 16)
                elif n < SELECTED_COUNT + 2:
                    half = n - SELECTED_COUNT
                    sp.dma_start(raw[:, buf, 0:WEIGHT_COLS], w1[:, WEIGHT_COLS * half:WEIGHT_COLS * (half + 1)]
                                 ).then_inc(raw_landed[buf], 16)
                else:
                    sp.dma_start(raw[:, buf, 0:N1 * HIDDEN2], w2).then_inc(raw_landed[buf], 16)
                if n == 1:
                    sp.dma_start(denseT[:], dense_t).then_inc(dense_landed, 16)
            sp.dma_start(b2_all[:], b2.broadcast_to([P, HIDDEN2])).then_inc(b2_landed, 16)
            sp.dma_start(w3_all[:], w3.broadcast_to([P, HIDDEN2])).then_inc(w3_landed, 16)
            out_by_tile = out.rearrange("(t p) o -> t p o", p=P)
            for t in range(TILES):
                sp.wait_ge(y_done, t + 1)
                sp.dma_start(out_by_tile[t], y[:, t:t + 1]).then_inc(stored[t], 16)
            for t in range(TILES):
                sp.wait_ge(stored[t], 16)

        @block.gpsimd
        def _(pool):
            nc.gpsimd.iota(partition[:], pattern=[[1, 1]], base=0, channel_multiplier=1,
                           allow_small_or_imprecise_dtypes=True).then_inc(partition_ready, 1)
            nc.gpsimd.memset(identity[:], 0.0).then_inc(identity_zeroed, 1)
            pool.wait_ge(identity_zeroed, 1)
            nc.gpsimd.affine_select(out=identity[:], in_=identity[:], compare_op=ALU.not_equal, fill=1.0, base=0,
                                    pattern=[[-1, P]], channel_multiplier=1).then_inc(identity_ready, 1)
            pool.wait_ge(idx_landed, 16)
            for t in range(TILES):
                for s, f in enumerate(GATHERED):
                    if t >= 1:
                        pool.wait_ge(rows_landed[s], 16 * t)
                    if t >= 2:
                        pool.wait_ge(rows_turned, GROUPS * (t - 2) + s // GROUP + 1)
                    pool.indirect_dma_start(
                        rows[:, t % 2, s, :], None, tables[f],
                        bass.IndirectOffsetOnAxis(ap=idx_sb[:, t, f:f + 1], axis=0)).then_inc(rows_landed[s], 16)

        def copy_diagonal(copy, n, samples):
            t, batch, half = n // BATCHES, n % BATCHES, n % 2
            for b in samples:
                src = gram[SLOTS * b:SLOTS * (b + 1), BATCH_BANKS * half:BATCH_BANKS * (half + 1),
                           0:PRODUCTS_PER_BANK * PRODUCT_COLS]
                src = src.rearrange("p k (g b j) -> p j k g b", g=PRODUCTS_PER_BANK, b=FOUR)[:, :, :, :, b]
                dst = diag[SLOTS * b:SLOTS * (b + 1), t % 2, :, BATCH_PRODUCTS * batch:BATCH_PRODUCTS * (batch + 1)]
                last = copy(dst.rearrange("p j (k g) -> p j k g", k=BATCH_BANKS), src)
            return last

        def pack_narrow(copy, t, columns):
            for j in columns:
                last = copy(packed[:, t % 2, packed_at(j):packed_at(j) + j], narrow[:, j - 1, 0:j])
            return last

        @block.scalar
        def _(act):
            def load_in(n):
                high, _, parts, cols = high_low(n)
                act.wait_ge(raw_landed[n % RAW_BUFFERS], raw_landed_at(n))
                if PART_BUFFERS <= n < SELECTED_COUNT:
                    act.wait_ge(chunk_selected, CHUNK0[n - PART_BUFFERS + 1])
                elif n >= SELECTED_COUNT:
                    act.wait_ge(chunk_selected, CHUNK0[SELECTED_COUNT])
                nc.scalar.copy(high, raw[0:parts, n % RAW_BUFFERS, 0:cols]).then_inc(load_high, 1)

            def ids_in(k):
                buf, at = k % IDS_BUFFERS, ROW0_AT[PLACES[k]]
                act.wait_ge(ids_landed[buf], 16 * (k // IDS_BUFFERS + 1))
                if k >= IDS_BUFFERS:
                    act.wait_ge(onehot_built, CHUNK0[k - IDS_BUFFERS + 1])
                nc.scalar.activation(ids_rel[0:SELECT_PARTS, buf, :], ids_all[0:SELECT_PARTS, buf, :], ACT.Identity,
                                     bias=minus_row0[0:SELECT_PARTS, at:at + 1]).then_inc(ids_rel_done, 1)

            for dst, src in table_parts(0):
                act.dma_start(dst, src).then_inc(raw_landed[0], 16)
            act.wait_ge(partition_ready, 1)
            for places, at in ROW0_AT.items():
                nc.scalar.activation(minus_row0[:, at:at + 1], partition[:], ACT.Identity,
                                     scale=-float(places)).then_inc(row0_ready, 1)
            act.wait_ge(row0_ready, len(ROW0_AT))
            for k in range(AHEAD):
                ids_in(k)
                load_in(k)
            for step, n in SCHEDULE:
                if step == "select":
                    if n + AHEAD < SELECTED_COUNT:
                        ids_in(n + AHEAD)
                        load_in(n + AHEAD)
                    act.wait_ge(chunk_selected, CHUNK0[n + 1])
                    nc.scalar.copy(slot_view(SELECT_SLOT0 + n), by_sample(sums[:, n % 2, :])
                                   ).then_inc(selected_copied, 1)
                elif step == "dense_in":
                    act.wait_ge(dense_landed, 16)
                    nc.scalar.copy(dense_h[:], denseT[:]).then_inc(dense_high, 1)
                elif step == "weights_in":
                    load_in(SELECTED_COUNT + n)
                elif step == "rows":
                    slots = group_slots(n)
                    act.wait_ge(rows_turned, n + 1)
                    dst = featT[:, n // GROUPS, :, :, slots[0]:slots[-1] + 1]
                    nc.scalar.copy(dst.rearrange("p g b f -> p f b g"),
                                   rowsT[:, 0:len(slots), :].rearrange("p f (b g) -> p f b g", b=FOUR)
                                   ).then_inc(rows_copied, 1)
                elif step == "products":
                    act.wait_ge(products_done, n + 1)
                    if n // BATCHES >= 2:
                        act.wait_ge(narrow_turned, n // BATCHES - 1)
                    copy_diagonal(nc.scalar.copy, n, (2, 3)).then_inc(diag_by_act, 1)
                elif step == "pack":
                    act.wait_ge(narrow_turned, n + 1)
                    act.wait_ge(wide_turned, n + 1)
                    pack_narrow(nc.scalar.copy, n, range(1, HALF, 2)).then_inc(packed_by_act, 1)
                elif step == "pairsT":
                    act.wait_ge(pairs_turned, n + 1)
                    if n >= 1:
                        act.wait_ge(h1_summed, n)
                    nc.scalar.copy(pairs_h[:], mlpT[:, 0:PAIR_CHUNKS, :]).then_inc(pairs_high, 1)
                elif step == "layer1":
                    act.wait_ge(h1_summed, n + 1)
                    if n >= 1:
                        act.wait_ge(h1_turned, n)
                    nc.scalar.activation(h1[:].rearrange("p c b -> p (c b)"), sums[:, 0, :],
                                         ACT.Relu).then_inc(h1_done, 1)
                elif step == "hiddenT":
                    act.wait_ge(h1_turned, n + 1)
                    if n >= 1:
                        act.wait_ge(h2_summed, n)
                    nc.scalar.copy(h1T_h[:], mlpT[:]).then_inc(h1_high, 1)

        @block.vector
        def _(dve):
            def load_in(n):
                high, low, parts, cols = high_low(n)
                dve.wait_ge(load_high, n + 1)
                if PART_BUFFERS <= n < SELECTED_COUNT:
                    dve.wait_ge(chunk_selected, CHUNK0[n - PART_BUFFERS + 1])
                elif n >= SELECTED_COUNT:
                    dve.wait_ge(chunk_selected, CHUNK0[SELECTED_COUNT])
                nc.vector.tensor_tensor(low, raw[0:parts, n % RAW_BUFFERS, 0:cols], high.bitcast(fp32),
                                        ALU.subtract).then_inc(load_low, 1)

            def build_onehots(k, places):
                for c in places:
                    n = CHUNK0[k] + c
                    if n >= ONEHOTS:
                        dve.wait_ge(chunk_selected, n - ONEHOTS + 1)
                    nc.vector.tensor_scalar(onehot[0:SELECT_PARTS, n % ONEHOTS, :],
                                            ids_rel[0:SELECT_PARTS, k % IDS_BUFFERS, :], float(c), None,
                                            ALU.is_equal).then_inc(onehot_built, 1)

            nc.vector.memset(packed[:, :, BIAS_AT:], 0.0).then_inc(packed_set, 1)
            dve.wait_ge(packed_set, 1)
            nc.vector.memset(packed[:, :, BIAS_AT:BIAS_AT + 1], 1.0).then_inc(packed_set, 1)
            nc.vector.memset(featT[:].rearrange("p t g b s -> p (t g b) s")[:, :, FEATURES:SLOTS], 0.0).then_inc(padding_set, 1)
            for step, n in SCHEDULE:
                if step == "select":
                    dve.wait_ge(ids_rel_done, n + 1)
                    middle = PLACES[n] // 2
                    if n == 0:
                        build_onehots(0, range(1))
                        load_in(0)
                        build_onehots(0, range(1, middle))
                    else:
                        build_onehots(n, range(middle))
                    if n + 1 < SELECTED_COUNT:
                        load_in(n + 1)
                    build_onehots(n, range(middle, PLACES[n]))
                elif step == "dense_in":
                    dve.wait_ge(dense_high, 1)
                    nc.vector.tensor_copy(slot_view(DENSE_SLOT), by_sample(denseT[:])).then_inc(dense_copied, 1)
                    nc.vector.tensor_tensor(dense_l[:], denseT[:], dense_h[:].bitcast(fp32),
                                            ALU.subtract).then_inc(dense_low, 1)
                elif step == "weights_in":
                    load_in(SELECTED_COUNT + n)
                elif step == "products":
                    dve.wait_ge(products_done, n + 1)
                    if n // BATCHES >= 2:
                        dve.wait_ge(narrow_turned, n // BATCHES - 1)
                    copy_diagonal(nc.vector.tensor_copy, n, (0, 1)).then_inc(diag_by_dve, 1)
                elif step == "pack":
                    dve.wait_ge(diag_by_dve, BATCHES * (n + 1))
                    dve.wait_ge(diag_by_act, BATCHES * (n + 1))
                    if n >= 2:
                        dve.wait_ge(pairs_turned, n - 1)
                    nc.vector.transpose(packed[:, n % 2, 0:BIAS_AT],
                                        diag[:, n % 2, HALF - 1:, :].rearrange("p j g -> p (j g)")
                                        ).then_inc(wide_turned, 1)
                    if n >= 1:
                        dve.wait_ge(packed_by_act, n)
                        dve.wait_ge(packed_by_dve, n)
                    nc.vector.transpose(narrow[:].rearrange("p j i -> p (j i)"),
                                        diag[:, n % 2, 0:HALF - 1, :].rearrange("p j g -> p (j g)")
                                        ).then_inc(narrow_turned, 1)
                    dve.wait_ge(wide_turned, n + 1)
                    dve.wait_ge(narrow_turned, n + 1)
                    pack_narrow(nc.vector.tensor_copy, n, range(2, HALF, 2)).then_inc(packed_by_dve, 1)
                elif step == "pairsT":
                    dve.wait_ge(pairs_high, n + 1)
                    if n >= 1:
                        dve.wait_ge(h1_summed, n)
                    nc.vector.tensor_tensor(pairs_l[:], mlpT[:, 0:PAIR_CHUNKS, :], pairs_h[:].bitcast(fp32),
                                            ALU.subtract).then_inc(pairs_low, 1)
                elif step == "hiddenT":
                    dve.wait_ge(h1_high, n + 1)
                    if n >= 1:
                        dve.wait_ge(h2_summed, n)
                    nc.vector.tensor_tensor(h1T_l[:], mlpT[:], h1T_h[:].bitcast(fp32),
                                            ALU.subtract).then_inc(h1_low, 1)
                elif step == "layer2":
                    if n == 0:
                        dve.wait_ge(b2_landed, 16)
                        dve.wait_ge(w3_landed, 16)
                    else:
                        dve.wait_ge(y_done, n)
                    dve.wait_ge(h2_summed, n + 1)
                    nc.vector.tensor_tensor(h2[:], sums[:, 1, 0:HIDDEN2], b2_all[:], ALU.add).then_inc(h2_biased, 1)
                    dve.wait_ge(h2_biased, n + 1)
                    nc.vector.scalar_tensor_tensor(h2_w3[:], h2[:], 0.0, w3_all[:], ALU.max, ALU.mult,
                                                   accum_out=y[:, n:n + 1]).then_inc(y_done, 1)

        @block.tensor
        def _(pe):
            def passes(dst, chunks, left_h, left_l, right_h, right_l, low_ready, first=True, last=True):
                for c in chunks:
                    nc.tensor.matmul(dst, left_h[:, c, :], right_h[:, c, :], start=first and c == chunks[0], stop=False)
                    nc.tensor.matmul(dst, left_h[:, c, :], right_l[:, c, :], start=False, stop=False)
                pe.wait_ge(*low_ready)
                for c in chunks:
                    end = nc.tensor.matmul(dst, left_l[:, c, :], right_h[:, c, :], start=False,
                                           stop=last and c == chunks[-1])
                return end

            for step, n in SCHEDULE:
                if step == "select":
                    pe.wait_ge(load_low, n + 1)
                    if n >= 2:
                        pe.wait_ge(selected_copied, n - 1)
                    for c in range(PLACES[n]):
                        m = CHUNK0[n] + c
                        pe.wait_ge(onehot_built, m + 1)
                        hot = onehot[0:SELECT_PARTS, m % ONEHOTS, :]
                        nc.tensor.matmul(sums[:, n % 2, :], table_h[0:SELECT_PARTS, n % PART_BUFFERS, c, :], hot,
                                         start=(c == 0), stop=False)
                        nc.tensor.matmul(sums[:, n % 2, :], table_l[0:SELECT_PARTS, n % PART_BUFFERS, c, :], hot,
                                         start=False, stop=(c == PLACES[n] - 1)).then_inc(chunk_selected, 1)
                elif step == "rows":
                    t = n // GROUPS
                    if n == 0:
                        pe.wait_ge(identity_ready, 1)
                    else:
                        pe.wait_ge(rows_copied, n)
                    for i, s in enumerate(group_slots(n)):
                        pe.wait_ge(rows_landed[s], 16 * (t + 1))
                        last = nc.tensor.transpose(rowsT[:, i, :], rows[:, t % 2, s, :], identity[:])
                    last.then_inc(rows_turned, 1)
                elif step == "products":
                    t, batch = divmod(n, BATCHES)
                    if n == 0:
                        pe.wait_ge(selected_copied, SELECTED_COUNT)
                        pe.wait_ge(dense_copied, 1)
                        pe.wait_ge(padding_set, 1)
                    if batch == 0:
                        pe.wait_ge(rows_copied, GROUPS * (t + 1))
                    if n >= 2:
                        pe.wait_ge(diag_by_dve, n - 1)
                        pe.wait_ge(diag_by_act, n - 1)
                    for m in range(BATCH_PRODUCTS):
                        four = featT[:, t, BATCH_PRODUCTS * batch + m]
                        col = PRODUCT_COLS * (m % PRODUCTS_PER_BANK)
                        dst = gram[:, BATCH_BANKS * (n % 2) + m // PRODUCTS_PER_BANK, col:col + PRODUCT_COLS]
                        last = nc.tensor.matmul(dst, four.rearrange("p b s -> p (b s)"), four[:, :, 1:FEATURES], start=True, stop=True)
                    last.then_inc(products_done, 1)
                elif step == "dense":
                    if n == 0:
                        pe.wait_ge(dense_low, 1)
                        pe.wait_ge(load_low, SELECTED_COUNT + 2)
                    else:
                        pe.wait_ge(h1_done, n)
                    w = [x[:, DENSE_CHUNK, :] for x in (w1_h, w1_l)]
                    d = [x[:, P * n:P * (n + 1)] for x in (dense_h, dense_l)]
                    for part, (left, right) in enumerate(((d[0], w[0]), (d[0], w[1]), (d[1], w[0]))):
                        nc.tensor.matmul(sums[:, 0, :], left, right, start=(part == 0), stop=False)
                elif step == "pairsT":
                    pe.wait_ge(packed_by_dve, n + 1)
                    pe.wait_ge(packed_by_act, n + 1)
                    if n == 0:
                        pe.wait_ge(packed_set, 2)
                    else:
                        pe.wait_ge(h1_low, n)
                    for c in range(PAIR_CHUNKS):
                        last = nc.tensor.transpose(mlpT[:, c, :], packed[:, n % 2, P * c:P * (c + 1)], identity[:])
                    last.then_inc(pairs_turned, 1)
                elif step == "layer1":
                    pe.wait_ge(pairs_high, n + 1)
                    passes(sums[:, 0, :], range(PAIR_CHUNKS), pairs_h, pairs_l, w1_h, w1_l,
                           low_ready=(pairs_low, n + 1), first=False).then_inc(h1_summed, 1)
                elif step == "hiddenT":
                    pe.wait_ge(h1_done, n + 1)
                    for c in range(N1):
                        last = nc.tensor.transpose(mlpT[:, c, :], h1[:, c, :], identity[:])
                    last.then_inc(h1_turned, 1)
                elif step == "layer2":
                    if n == 0:
                        pe.wait_ge(load_low, LOADS)
                    else:
                        pe.wait_ge(h2_biased, n)
                    pe.wait_ge(h1_high, n + 1)
                    passes(sums[:, 1, 0:HIDDEN2], range(N1), h1T_h, h1T_l, w2_h, w2_l,
                           low_ready=(h1_low, n + 1)).then_inc(h2_summed, 1)


def pair_row(a, b):
    return a * (FEATURES - 1) - a * (a - 1) // 2 + (b - a - 1)


def arrange_w1(w, b):
    arranged = np.zeros((CHUNKS1 * P, HIDDEN1), w.dtype)
    for j in range(1, FEATURES):
        for i in range(j):
            arranged[packed_at(j) + i] = w[pair_row(*sorted((SLOT_FEATURE[i], SLOT_FEATURE[j])))]
    arranged[BIAS_AT] = b
    arranged[DENSE_CHUNK * P:] = w[FEATURES * (FEATURES - 1) // 2:]
    return arranged.reshape(CHUNKS1, P, HIDDEN1).transpose(1, 0, 2).reshape(P, CHUNKS1 * HIDDEN1)


def kernel(**inputs):
    import concourse.bacc as bacc
    from concourse.bass_utils import run_bass_kernel_spmd

    ids, dense = np.asarray(inputs["ids"]), np.asarray(inputs["r_dense"])
    w2 = np.asarray(inputs["W_top2"])
    host = {
        "idx": ids.reshape(TILES, P, TABLES).transpose(1, 0, 2).reshape(P, TILES * TABLES),
        "ids_by_table": ids.T[SELECTED],
        "dense_t": dense.T,
        **{f"tbl_{f}": np.asarray(inputs[f"tbl_{f}"]) for f in range(TABLES)},
        "w1": arrange_w1(np.asarray(inputs["W_top1"]), np.asarray(inputs["b_top1"])),
        "w2": w2.reshape(N1, P, HIDDEN2).transpose(1, 0, 2).reshape(P, N1 * HIDDEN2),
        "b2": np.asarray(inputs["b_top2"]).reshape(1, HIDDEN2),
        "w3": np.asarray(inputs["W_top3"]).reshape(1, HIDDEN2),
    }
    host = {name: np.ascontiguousarray(a) for name, a in host.items()}
    nc = bacc.Bacc("TRN2", target_bir_lowering=False, num_devices=1)
    aps = {name: nc.dram_tensor(name, a.shape, mybir.dt.from_np(a.dtype), kind="ExternalInput").ap()
           for name, a in host.items()}
    out = nc.dram_tensor("y_out", (B, 1), mybir.dt.float32, kind="ExternalOutput").ap()
    build(nc, aps["idx"], aps["ids_by_table"], aps["dense_t"], [aps[f"tbl_{f}"] for f in range(TABLES)],
          aps["w1"], aps["w2"], aps["b2"], aps["w3"], out)
    return run_bass_kernel_spmd(nc, [host], core_ids=[0]).results[0]["y_out"]
```

```python
import numpy as np

import concourse.bass as bass
from concourse import mybir
from contextlib import ExitStack

P = 128
B = 512
D = 128
TILES = B // P
ROWS = [1250, 12500, 125000, 1000, 1250, 12500, 1250, 12500, 1000, 1000, 12500, 1000, 12500,
        1000, 1250, 1250, 1250, 12500, 1000, 1250, 12500, 1250, 1250, 1250, 12500, 1250]
TABLES = len(ROWS)
FEATURES = TABLES + 1
HIDDEN1, HIDDEN2 = 512, 256
N1 = HIDDEN1 // P

SELECT_PARTS = 125
SELECTED_COUNT = 9
SELECTED = sorted((f for f in range(TABLES) if ROWS[f] <= 1250), key=lambda f: ROWS[f])[:SELECTED_COUNT]
GATHERED = [f for f in range(TABLES) if f not in SELECTED]
PLACES = [ROWS[f] // SELECT_PARTS for f in SELECTED]
MAX_PLACES = max(PLACES)
CHUNK0 = [sum(PLACES[:k]) for k in range(SELECTED_COUNT + 1)]
ROW0_AT = {n: at for at, n in enumerate(sorted(set(PLACES)))}
GROUP = 4
GROUPS = -(-len(GATHERED) // GROUP)

SLOTS = 32
SLOT_FEATURE = [f + 1 for f in GATHERED] + [f + 1 for f in SELECTED] + [0]
DENSE_SLOT = FEATURES - 1
SELECT_SLOT0 = len(GATHERED)

MOVING = FEATURES - 1
FOUR = P // SLOTS
BATCH = 8
BATCHES = P // (BATCH * FOUR)
GRAM_BANKS = 4

HALF = SLOTS // 2
WIDE = MOVING - HALF + 1
NARROW = HALF - 1
TAIL_COLUMNS = HALF - WIDE
BIAS_AT = WIDE * SLOTS
PACKED = 3 * P
assert BIAS_AT < PACKED and TAIL_COLUMNS * (TAIL_COLUMNS + 1) // 2 <= HALF


def packed_at(j):
    if j >= HALF:
        return SLOTS * (j - HALF)
    if j > TAIL_COLUMNS:
        w = HALF - j
        return SLOTS * w + HALF + w
    return HALF + j * (j - 1) // 2


PAIR_CHUNKS = PACKED // P
DENSE_CHUNK = PAIR_CHUNKS
CHUNKS1 = PAIR_CHUNKS + 1

WARM_UP_PRODUCTS = 11
ONEHOTS = 12
IDS_BUFFERS = 3
PART_BUFFERS = 3
AHEAD = 2
RAW_BUFFERS = 3
WEIGHT_LOADS = 3
W1_HALVES = 1, 0
WEIGHT_COLS = CHUNKS1 * HIDDEN1 // 2
LOADS = SELECTED_COUNT + WEIGHT_LOADS
EARLY = 2 * P
LATE_PARTS = 2
DIRECT = 3
PIECES = 2
PIECE_CHUNKS = 2


def piece(p, chunks):
    return range(PIECE_CHUNKS * p, min(PIECE_CHUNKS * (p + 1), chunks))


def raw_landed_at(n):
    return sum(32 if m < SELECTED_COUNT else 16 for m in range(n % RAW_BUFFERS, n + 1, RAW_BUFFERS))


def late_places(part):
    return range(PLACES[-1] * part // LATE_PARTS, PLACES[-1] * (part + 1) // LATE_PARTS)


def schedule():
    order = [("keep_warm", WARM_UP_PRODUCTS)]
    for k in range(SELECTED_COUNT):
        if k == 1:
            order.append(("dense_high", 0))
        order += [("select", k), ("rows", 1 if k < 2 * GROUPS else 0)]
    P0, P1, P2, P3 = ([("products", BATCHES * t + n) for n in range(BATCHES)] for t in range(TILES))
    row, more_rows = ("rows", 1), ("rows", GROUPS - BATCHES)
    order += [
        ("weights_in", 0), ("dense_low", 0),
        P0[0], ("select_late", 0), row, ("weights_in", 1),
        P0[1], ("select_late", 1), more_rows,
        P0[2], P0[3], ("pack", 0), P1[0], row,
        P1[1], ("dense", 0), ("pack_act", 0), ("weights_in", 2), row, ("pairsT", 0),
        P1[2], ("layer1", 0), row,
        P1[3], row, ("hiddenT", 0), ("pack", 1),
        P2[0], ("pack_act", 1), ("layer2", 0), ("dense", 1), row, ("pairsT", 1),
        P2[1], ("layer1", 1), row,
        P2[2], ("hiddenT", 1), row,
        P2[3], ("pack", 2), ("layer2", 1), ("dense", 2), ("pack_act", 2), ("keep_warm", 5), ("pairsT", 2), row,
        ("layer1", 2), more_rows, ("hiddenT", 2),
        P3[0], P3[1], ("keep_warm", 1), P3[2], P3[3], ("pack", 3), ("pack_act", 3), ("layer2", 2), ("dense", 3), ("keep_warm", 4),
        ("pairsT", 3), ("keep_warm", 3), ("layer1", 3), ("keep_warm", 2), ("hiddenT", 3), ("keep_warm", 2),
        ("layer2", 3),
    ]
    group = 0
    for step, n in order:
        if step == "rows":
            for group in range(group, group + n):
                yield step, group
            group += n > 0
        else:
            yield step, n


SCHEDULE = list(schedule())
assert [n for step, n in SCHEDULE if step == "rows"] == list(range(GROUPS * TILES))


def build(nc, idx, ids_by_table, dense_t, tables, w1, w2, b2, w3, out):
    fp32, fp32r, i32 = mybir.dt.float32, mybir.dt.float32r, mybir.dt.int32
    ALU, ACT = mybir.AluOpType, mybir.ActivationFunctionType

    with ExitStack() as ctx:
        def sb(name, shape, dt=fp32):
            return ctx.enter_context(nc.sbuf_tensor(name, shape, dt))

        def sem(name):
            return ctx.enter_context(nc.semaphore(name))

        idx_sb = sb("idx_sb", [P, TILES, TABLES], i32)
        ids_all = sb("ids_all", [P, IDS_BUFFERS, B], i32)
        ids_rel = sb("ids_rel", [P, IDS_BUFFERS, B])
        minus_row0 = sb("minus_row0", [P, len(ROW0_AT)])
        partition = sb("partition", [P, 1])
        identity = sb("identity", [P, P])
        raw = sb("raw", [P, RAW_BUFFERS, MAX_PLACES * D])
        table_h = sb("table_h", [P, PART_BUFFERS, MAX_PLACES, D], fp32r)
        table_l = sb("table_l", [P, PART_BUFFERS, MAX_PLACES, D], fp32r)
        onehot = sb("onehot", [P, ONEHOTS, B], fp32r)
        rows = sb("rows", [P, 2, len(GATHERED), D])
        featT = sb("featT", [P, TILES, P // FOUR, FOUR, SLOTS])
        denseT = sb("denseT", [P, B])
        dense_h = sb("dense_h", [P, B], fp32r)
        dense_l = sb("dense_l", [P, B], fp32r)
        products = sb("products", [P, 2, MOVING, SLOTS])
        narrow = sb("narrow", [P, NARROW, SLOTS])
        packed = sb("packed", [P, 2, PACKED])
        pairs_h = sb("pairs_h", [P, PAIR_CHUNKS, P], fp32r)
        pairs_l = sb("pairs_l", [P, PAIR_CHUNKS, P], fp32r)
        w1_h = sb("w1_h", [P, CHUNKS1, HIDDEN1], fp32r)
        w1_l = sb("w1_l", [P, CHUNKS1, HIDDEN1], fp32r)
        w2_h, w2_l = (onehot[:, at:at + N1 // 2, :].rearrange("p c (u n) -> p (c u) n", n=HIDDEN2)
                      for at in (0, N1 // 2))
        h1T_h, h1T_l = (onehot[:, at, :].rearrange("p (c b) -> p c b", b=P)
                        for at in (N1, N1 + 1))
        b2_all = sb("b2_all", [P, HIDDEN2])
        w3_all = sb("w3_all", [P, HIDDEN2])
        h1 = sb("h1", [P, HIDDEN1])
        h2 = sb("h2", [P, HIDDEN2])
        y = sb("y", [P, TILES])

        sums = ctx.enter_context(nc.psum_tensor("sums", [P, 2, 512], fp32))
        rowsT = ctx.enter_context(nc.psum_tensor("rowsT", [P, GROUP, P], fp32))
        mlpT = ctx.enter_context(nc.psum_tensor("mlpT", [P, 512], fp32))
        gram = ctx.enter_context(nc.psum_tensor("gram", [P, GRAM_BANKS, 512], fp32))

        idx_landed = sem("idx_landed")
        ids_landed = [sem(f"ids_landed{k}") for k in range(IDS_BUFFERS)]
        raw_landed = [sem(f"raw_landed{k}") for k in range(RAW_BUFFERS)]
        dense_landed = sem("dense_landed")
        b2_landed = sem("b2_landed")
        w3_landed = sem("w3_landed")
        rows_landed = [sem(f"rows_landed{s}") for s in range(len(GATHERED))]
        identity_zeroed = sem("identity_zeroed")
        identity_ready = sem("identity_ready")
        partition_ready = sem("partition_ready")
        row0_ready = sem("row0_ready")
        ids_rel_done = sem("ids_rel_done")
        padding_set = sem("padding_set")
        packed_set = sem("packed_set")
        load_high = sem("load_high")
        load_low = sem("load_low")
        dense_copied = sem("dense_copied")
        dense_high = sem("dense_high")
        dense_low = sem("dense_low")
        onehot_built = sem("onehot_built")
        chunk_selected = sem("chunk_selected")
        late_selected = sem("late_selected")
        late_copied = sem("late_copied")
        selected_copied = sem("selected_copied")
        rows_turned = sem("rows_turned")
        rows_copied = sem("rows_copied")
        products_done = sem("products_done")
        odd_copied = sem("odd_copied")
        even_copied = sem("even_copied")
        wide_turned = sem("wide_turned")
        narrow_turned = sem("narrow_turned")
        packed_by_dve = sem("packed_by_dve")
        packed_by_act = sem("packed_by_act")
        pairs_turned = sem("pairs_turned")
        pairs_high = sem("pairs_high")
        pairs_low = sem("pairs_low")
        h1_summed = sem("h1_summed")
        h1_done = sem("h1_done")
        h1_turned = sem("h1_turned")
        h1_high = sem("h1_high")
        h1_low = sem("h1_low")
        h2_summed = sem("h2_summed")
        h2_biased = sem("h2_biased")
        y_done = sem("y_done")
        stored = [sem(f"stored{t}") for t in range(TILES)]

        def slot_view(slot, samples=slice(0, B)):
            return featT[:, samples.start // P:samples.stop // P, :, :, slot].rearrange("p t g b -> p t b g")

        def by_sample(x):
            return x.rearrange("p (t b g) -> p t b g", b=FOUR, g=P // FOUR)

        def group_slots(m):
            return range(GROUP * (m % GROUPS), min(GROUP * (m % GROUPS) + GROUP, len(GATHERED)))

        def high_low(n):
            if n < SELECTED_COUNT:
                first = DIRECT if n == 0 else 0
                return [x[0:SELECT_PARTS, n % PART_BUFFERS, first:PLACES[n], :].rearrange("p r d -> p (r d)")
                        for x in (table_h, table_l)] + [SELECT_PARTS, first * D, PLACES[n] * D]
            n -= SELECTED_COUNT
            if n < 2:
                half = slice(W1_HALVES[n] * CHUNKS1 // 2, (W1_HALVES[n] + 1) * CHUNKS1 // 2)
                return [x[:, half, :].rearrange("p c n -> p (c n)") for x in (w1_h, w1_l)] + [P, 0, WEIGHT_COLS]
            return [x.rearrange("p c n -> p (c n)") for x in (w2_h, w2_l)] + [P, 0, N1 * HIDDEN2]

        def pairsT_piece(p):
            return (mlpT[:], sums[:, 1, :])[p][:, 0:P * len(piece(p, PAIR_CHUNKS))]

        def hiddenT_piece(p):
            return (mlpT[:], sums[:, 0, :])[p][:, 0:P * len(piece(p, N1))]

        def chunks_of(x, p, chunks):
            cs = piece(p, chunks)
            return x[:, cs[0]:cs[-1] + 1, :].rearrange("p c b -> p (c b)")

        def table_parts(n):
            cols = PLACES[n] * D
            src = tables[SELECTED[n]].rearrange("(p r) d -> p (r d)", r=PLACES[n])
            return [(raw[lo:hi, n % RAW_BUFFERS, 0:cols], src[lo:hi]) for lo, hi in ((0, 112), (112, SELECT_PARTS))]

        block = ctx.enter_context(nc.Block())

        @block.sync
        def _(sp):
            sp.dma_start(idx_sb[:], idx.rearrange("p (t f) -> p t f", t=TILES)).then_inc(idx_landed, 16)
            for n in range(LOADS):
                buf = n % RAW_BUFFERS
                if n < SELECTED_COUNT:
                    if n >= IDS_BUFFERS:
                        sp.wait_ge(ids_rel_done, n - IDS_BUFFERS + 1)
                    sp.dma_start(ids_all[:, n % IDS_BUFFERS, :], ids_by_table[n:n + 1, :].broadcast_to([P, B])
                                 ).then_inc(ids_landed[n % IDS_BUFFERS], 16)
                if n == 0:
                    continue
                if n >= RAW_BUFFERS:
                    sp.wait_ge(load_low, n - RAW_BUFFERS + 1)
                if n == RAW_BUFFERS:
                    sp.wait_ge(chunk_selected, DIRECT)
                if n < SELECTED_COUNT:
                    for dst, src in table_parts(n):
                        sp.dma_start(dst, src).then_inc(raw_landed[buf], 16)
                elif n < SELECTED_COUNT + 2:
                    half = W1_HALVES[n - SELECTED_COUNT]
                    sp.dma_start(raw[:, buf, 0:WEIGHT_COLS], w1[:, WEIGHT_COLS * half:WEIGHT_COLS * (half + 1)]
                                 ).then_inc(raw_landed[buf], 16)
                else:
                    sp.dma_start(raw[:, buf, 0:N1 * HIDDEN2], w2).then_inc(raw_landed[buf], 16)
                if n == 1:
                    sp.dma_start(denseT[:], dense_t).then_inc(dense_landed, 16)
            sp.dma_start(b2_all[:], b2.broadcast_to([P, HIDDEN2])).then_inc(b2_landed, 16)
            sp.dma_start(w3_all[:], w3.broadcast_to([P, HIDDEN2])).then_inc(w3_landed, 16)
            out_by_tile = out.rearrange("(t p) o -> t p o", p=P)
            for t in range(TILES):
                sp.wait_ge(y_done, t + 1)
                sp.dma_start(out_by_tile[t], y[:, t:t + 1]).then_inc(stored[t], 16)
            for t in range(TILES):
                sp.wait_ge(stored[t], 16)

        @block.gpsimd
        def _(pool):
            nc.gpsimd.iota(partition[:], pattern=[[1, 1]], base=0, channel_multiplier=1,
                           allow_small_or_imprecise_dtypes=True).then_inc(partition_ready, 1)
            nc.gpsimd.memset(identity[:], 0.0).then_inc(identity_zeroed, 1)
            pool.wait_ge(identity_zeroed, 1)
            nc.gpsimd.affine_select(out=identity[:], in_=identity[:], compare_op=ALU.not_equal, fill=1.0, base=0,
                                    pattern=[[-1, P]], channel_multiplier=1).then_inc(identity_ready, 1)
            pool.wait_ge(idx_landed, 16)
            for t in range(TILES):
                for s, f in enumerate(GATHERED):
                    if t >= 1:
                        pool.wait_ge(rows_landed[s], 16 * t)
                    if t >= 2:
                        pool.wait_ge(rows_turned, GROUPS * (t - 2) + s // GROUP + 1)
                    pool.indirect_dma_start(
                        rows[:, t % 2, s, :], None, tables[f],
                        bass.IndirectOffsetOnAxis(ap=idx_sb[:, t, f:f + 1], axis=0)).then_inc(rows_landed[s], 16)

        def copy_batch(copy, n):
            t, batch = divmod(n, BATCHES)
            src = gram[:, n % GRAM_BANKS, 0:BATCH * MOVING].rearrange("p (g j) -> p j g", g=BATCH)
            return copy(products[:, t % 2, :, BATCH * batch:BATCH * (batch + 1)], src)

        def pack_narrow(copy, t, columns):
            for j in columns:
                last = copy(packed[:, t % 2, packed_at(j):packed_at(j) + j], narrow[:, j - 1, 0:j])
            return last

        @block.scalar
        def _(act):
            def load_in(n):
                high, _, parts, first, cols = high_low(n)
                act.wait_ge(raw_landed[n % RAW_BUFFERS], raw_landed_at(n))
                if PART_BUFFERS <= n < SELECTED_COUNT:
                    act.wait_ge(chunk_selected, CHUNK0[n - PART_BUFFERS + 1])
                elif n == LOADS - 1:
                    act.wait_ge(late_selected, PLACES[-1])
                nc.scalar.copy(high, raw[0:parts, n % RAW_BUFFERS, first:cols]).then_inc(load_high, 1)

            def ids_in(k):
                buf, at = k % IDS_BUFFERS, ROW0_AT[PLACES[k]]
                act.wait_ge(ids_landed[buf], 16 * (k // IDS_BUFFERS + 1))
                if k >= IDS_BUFFERS:
                    act.wait_ge(onehot_built, CHUNK0[k - IDS_BUFFERS + 1])
                nc.scalar.activation(ids_rel[0:SELECT_PARTS, buf, :], ids_all[0:SELECT_PARTS, buf, :], ACT.Identity,
                                     bias=minus_row0[0:SELECT_PARTS, at:at + 1]).then_inc(ids_rel_done, 1)

            for dst, src in table_parts(0):
                act.dma_start(dst, src).then_inc(raw_landed[0], 16)
            act.wait_ge(partition_ready, 1)
            for places, at in ROW0_AT.items():
                nc.scalar.activation(minus_row0[:, at:at + 1], partition[:], ACT.Identity,
                                     scale=-float(places)).then_inc(row0_ready, 1)
            act.wait_ge(row0_ready, len(ROW0_AT))
            for k in range(AHEAD):
                ids_in(k)
                load_in(k)
            for step, n in SCHEDULE:
                if step == "select":
                    if n + AHEAD < SELECTED_COUNT:
                        ids_in(n + AHEAD)
                        load_in(n + AHEAD)
                    act.wait_ge(chunk_selected, CHUNK0[n + 1])
                    samples = slice(0, B if n < SELECTED_COUNT - 1 else EARLY)
                    nc.scalar.copy(slot_view(SELECT_SLOT0 + n, samples), by_sample(sums[:, n % 2, samples])
                                   ).then_inc(selected_copied, 1)
                elif step == "select_late" and n == LATE_PARTS - 1:
                    act.wait_ge(late_selected, PLACES[-1])
                    nc.scalar.copy(slot_view(SELECT_SLOT0 + SELECTED_COUNT - 1, slice(EARLY, B)),
                                   by_sample(sums[:, SELECTED_COUNT % 2, EARLY:B])).then_inc(late_copied, 1)
                elif step == "dense_high":
                    act.wait_ge(dense_landed, 16)
                    nc.scalar.copy(dense_h[:], denseT[:]).then_inc(dense_high, 1)
                    nc.scalar.copy(slot_view(DENSE_SLOT), by_sample(denseT[:])).then_inc(dense_copied, 1)
                elif step == "weights_in":
                    load_in(SELECTED_COUNT + n)
                elif step == "rows":
                    slots = group_slots(n)
                    act.wait_ge(rows_turned, n + 1)
                    dst = featT[:, n // GROUPS, :, :, slots[0]:slots[-1] + 1]
                    nc.scalar.copy(dst.rearrange("p g b f -> p f b g"),
                                   rowsT[:, 0:len(slots), :].rearrange("p f (b g) -> p f b g", b=FOUR)
                                   ).then_inc(rows_copied, 1)
                elif step == "products":
                    if n % 2 == 0:
                        act.wait_ge(products_done, n + 1)
                        if n // BATCHES >= 2:
                            act.wait_ge(narrow_turned, n // BATCHES - 1)
                        copy_batch(nc.scalar.copy, n).then_inc(even_copied, 1)
                elif step == "pack_act":
                    act.wait_ge(narrow_turned, n + 1)
                    act.wait_ge(wide_turned, n + 1)
                    pack_narrow(nc.scalar.copy, n, range(2, HALF, 2)).then_inc(packed_by_act, 1)
                elif step == "pairsT":
                    if n >= 1:
                        act.wait_ge(h1_summed, n)
                    for p in range(PIECES):
                        act.wait_ge(pairs_turned, PIECES * n + p + 1)
                        nc.scalar.copy(chunks_of(pairs_h, p, PAIR_CHUNKS), pairsT_piece(p)).then_inc(pairs_high, 1)
                elif step == "layer1":
                    act.wait_ge(h1_summed, n + 1)
                    if n >= 1:
                        act.wait_ge(h1_turned, PIECES * n)
                    for p in range(PIECES):
                        cols = slice(HIDDEN1 // PIECES * p, HIDDEN1 // PIECES * (p + 1))
                        nc.scalar.activation(h1[:, cols], sums[:, 0, cols], ACT.Relu).then_inc(h1_done, 1)
                elif step == "hiddenT":
                    if n >= 1:
                        act.wait_ge(h2_summed, n)
                    for p in range(PIECES):
                        act.wait_ge(h1_turned, PIECES * n + p + 1)
                        nc.scalar.copy(chunks_of(h1T_h, p, N1), hiddenT_piece(p)).then_inc(h1_high, 1)

        @block.vector
        def _(dve):
            def load_in(n):
                high, low, parts, first, cols = high_low(n)
                if PART_BUFFERS <= n < SELECTED_COUNT:
                    dve.wait_ge(chunk_selected, CHUNK0[n - PART_BUFFERS + 1])
                elif n == LOADS - 1:
                    dve.wait_ge(late_selected, PLACES[-1])
                dve.wait_ge(load_high, n + 1)
                nc.vector.tensor_tensor(low, raw[0:parts, n % RAW_BUFFERS, first:cols], high.bitcast(fp32),
                                        ALU.subtract).then_inc(load_low, 1)

            def build_onehots(k, places):
                for c in places:
                    n = CHUNK0[k] + c
                    if n >= ONEHOTS:
                        dve.wait_ge(chunk_selected, n - ONEHOTS + 1)
                    nc.vector.tensor_scalar(onehot[0:SELECT_PARTS, n % ONEHOTS, :],
                                            ids_rel[0:SELECT_PARTS, k % IDS_BUFFERS, :], float(c), None,
                                            ALU.is_equal).then_inc(onehot_built, 1)

            nc.vector.memset(packed[:, :, BIAS_AT:], 0.0).then_inc(packed_set, 1)
            dve.wait_ge(packed_set, 1)
            nc.vector.memset(packed[:, :, BIAS_AT:BIAS_AT + 1], 1.0).then_inc(packed_set, 1)
            nc.vector.memset(featT[:].rearrange("p t g b s -> p (t g b) s")[:, :, FEATURES:SLOTS], 0.0
                             ).then_inc(padding_set, 1)
            for step, n in SCHEDULE:
                if step == "select":
                    dve.wait_ge(ids_rel_done, n + 1)
                    middle = PLACES[n] // 2
                    build_onehots(n, range(middle))
                    if n == 0:
                        load_in(0)
                    if n + 1 < SELECTED_COUNT:
                        load_in(n + 1)
                    build_onehots(n, range(middle, PLACES[n]))
                elif step == "dense_low":
                    dve.wait_ge(dense_high, 1)
                    nc.vector.tensor_tensor(dense_l[:], denseT[:], dense_h[:].bitcast(fp32),
                                            ALU.subtract).then_inc(dense_low, 1)
                elif step == "weights_in":
                    load_in(SELECTED_COUNT + n)
                elif step == "products":
                    if n % 2 == 1:
                        dve.wait_ge(products_done, n + 1)
                        if n // BATCHES >= 2:
                            dve.wait_ge(narrow_turned, n // BATCHES - 1)
                        copy_batch(nc.vector.tensor_copy, n).then_inc(odd_copied, 1)
                elif step == "pack":
                    dve.wait_ge(even_copied, BATCHES // 2 * (n + 1))
                    dve.wait_ge(odd_copied, BATCHES // 2 * (n + 1))
                    if n >= 2:
                        dve.wait_ge(pairs_turned, PIECES * (n - 1))
                    nc.vector.transpose(packed[:, n % 2, 0:BIAS_AT],
                                        products[:, n % 2, HALF - 1:, :].rearrange("p j g -> p (j g)")
                                        ).then_inc(wide_turned, 1)
                    if n >= 1:
                        dve.wait_ge(packed_by_act, n)
                        dve.wait_ge(packed_by_dve, n)
                    nc.vector.transpose(narrow[:].rearrange("p j i -> p (j i)"),
                                        products[:, n % 2, 0:HALF - 1, :].rearrange("p j g -> p (j g)")
                                        ).then_inc(narrow_turned, 1)
                    dve.wait_ge(wide_turned, n + 1)
                    dve.wait_ge(narrow_turned, n + 1)
                    pack_narrow(nc.vector.tensor_copy, n, range(1, HALF, 2)).then_inc(packed_by_dve, 1)
                elif step == "pairsT":
                    if n >= 1:
                        dve.wait_ge(h1_summed, n)
                    for p in range(PIECES):
                        dve.wait_ge(pairs_high, PIECES * n + p + 1)
                        nc.vector.tensor_tensor(chunks_of(pairs_l, p, PAIR_CHUNKS), pairsT_piece(p),
                                                chunks_of(pairs_h, p, PAIR_CHUNKS).bitcast(fp32),
                                                ALU.subtract).then_inc(pairs_low, 1)
                elif step == "hiddenT":
                    if n >= 1:
                        dve.wait_ge(h2_summed, n)
                    for p in range(PIECES):
                        dve.wait_ge(h1_high, PIECES * n + p + 1)
                        nc.vector.tensor_tensor(chunks_of(h1T_l, p, N1), hiddenT_piece(p),
                                                chunks_of(h1T_h, p, N1).bitcast(fp32), ALU.subtract).then_inc(h1_low, 1)
                elif step == "layer2":
                    if n == 0:
                        dve.wait_ge(b2_landed, 16)
                        dve.wait_ge(w3_landed, 16)
                    else:
                        dve.wait_ge(y_done, n)
                    dve.wait_ge(h2_summed, n + 1)
                    nc.vector.tensor_tensor(h2[:], sums[:, 1, 0:HIDDEN2], b2_all[:], ALU.add).then_inc(h2_biased, 1)
                    dve.wait_ge(h2_biased, n + 1)
                    nc.vector.scalar_tensor_tensor(h2[:], h2[:], 0.0, w3_all[:], ALU.max, ALU.mult,
                                                   accum_out=y[:, n:n + 1]).then_inc(y_done, 1)

        @block.tensor
        def _(pe):
            def passes(dst, tile, chunks, left_h, left_l, right_h, right_l, high_ready, low_ready, first=True):
                for p in range(PIECES):
                    pe.wait_ge(high_ready, PIECES * tile + p + 1)
                    for c in piece(p, chunks):
                        nc.tensor.matmul(dst, left_h[:, c, :], right_h[:, c, :], start=first and c == 0, stop=False)
                        nc.tensor.matmul(dst, left_h[:, c, :], right_l[:, c, :], start=False, stop=False)
                for p in range(PIECES):
                    pe.wait_ge(low_ready, PIECES * tile + p + 1)
                    for c in piece(p, chunks):
                        end = nc.tensor.matmul(dst, left_l[:, c, :], right_h[:, c, :], start=False,
                                               stop=(c == chunks - 1))
                return end

            groups_turned = 0
            for step, n in SCHEDULE:
                if step == "keep_warm":
                    if groups_turned == 0:
                        pe.wait_ge(identity_ready, 1)
                    else:
                        pe.wait_ge(rows_copied, groups_turned)
                    for _ in range(n):
                        nc.tensor.matmul(rowsT[:, 0, :], identity[:], identity[:], start=True, stop=True)
                elif step == "select":
                    if n >= 1:
                        pe.wait_ge(load_low, n + 1)
                    if n >= 2:
                        pe.wait_ge(selected_copied, n - 1)
                    for c in range(PLACES[n]):
                        m = CHUNK0[n] + c
                        samples = slice(0, B if n < SELECTED_COUNT - 1 else EARLY)
                        dst, hot = sums[:, n % 2, samples], onehot[0:SELECT_PARTS, m % ONEHOTS, samples]
                        if m == 0:
                            pe.wait_ge(raw_landed[0], raw_landed_at(0))
                        if m == DIRECT:
                            pe.wait_ge(load_low, 1)
                        pe.wait_ge(onehot_built, m + 1)
                        if m < DIRECT:
                            nc.tensor.matmul(dst, raw[0:SELECT_PARTS, 0, D * c:D * (c + 1)], hot.bitcast(fp32),
                                             start=(c == 0), stop=False).then_inc(chunk_selected, 1)
                        else:
                            nc.tensor.matmul(dst, table_h[0:SELECT_PARTS, n % PART_BUFFERS, c, :], hot,
                                             start=(c == 0), stop=False)
                            nc.tensor.matmul(dst, table_l[0:SELECT_PARTS, n % PART_BUFFERS, c, :], hot,
                                             start=False, stop=(c == PLACES[n] - 1)).then_inc(chunk_selected, 1)
                elif step == "select_late":
                    if n == 0:
                        pe.wait_ge(selected_copied, SELECTED_COUNT - 1)
                    for c in late_places(n):
                        hot = onehot[0:SELECT_PARTS, (CHUNK0[-2] + c) % ONEHOTS, EARLY:B]
                        dst = sums[:, SELECTED_COUNT % 2, EARLY:B]
                        for part in (table_h, table_l):
                            last = nc.tensor.matmul(
                                dst, part[0:SELECT_PARTS, (SELECTED_COUNT - 1) % PART_BUFFERS, c, :], hot,
                                start=(c == 0 and part is table_h), stop=(c == PLACES[-1] - 1 and part is table_l))
                        last.then_inc(late_selected, 1)
                elif step == "rows":
                    t = n // GROUPS
                    if n == 0:
                        pe.wait_ge(identity_ready, 1)
                    else:
                        pe.wait_ge(rows_copied, n)
                    for i, s in enumerate(group_slots(n)):
                        pe.wait_ge(rows_landed[s], 16 * (t + 1))
                        last = nc.tensor.transpose(rowsT[:, i, :], rows[:, t % 2, s, :], identity[:])
                    last.then_inc(rows_turned, 1)
                    groups_turned = n + 1
                elif step == "products":
                    t, batch = divmod(n, BATCHES)
                    if n == 0:
                        pe.wait_ge(selected_copied, SELECTED_COUNT)
                        pe.wait_ge(dense_copied, 1)
                        pe.wait_ge(padding_set, 1)
                    if n == BATCHES * EARLY // P:
                        pe.wait_ge(late_copied, 1)
                    if batch == 0:
                        pe.wait_ge(rows_copied, GROUPS * (t + 1))
                    if n >= GRAM_BANKS:
                        last_batch = n - GRAM_BANKS
                        pe.wait_ge((even_copied, odd_copied)[last_batch % 2], last_batch // 2 + 1)
                    for m in range(BATCH):
                        for b in range(FOUR):
                            sample = featT[:, t, BATCH * batch + m, b]
                            last = nc.tensor.matmul(
                                gram[SLOTS * b:SLOTS * (b + 1), n % GRAM_BANKS, MOVING * m:MOVING * (m + 1)],
                                sample, sample[:, 1:FEATURES], start=True, stop=True)
                    last.then_inc(products_done, 1)
                elif step == "dense":
                    if n == 0:
                        pe.wait_ge(dense_low, 1)
                        pe.wait_ge(load_low, SELECTED_COUNT + 1)
                    else:
                        pe.wait_ge(h1_low, PIECES * n)
                    w = [x[:, DENSE_CHUNK, :] for x in (w1_h, w1_l)]
                    d = [x[:, P * n:P * (n + 1)] for x in (dense_h, dense_l)]
                    for part, (left, right) in enumerate(((d[0], w[0]), (d[0], w[1]), (d[1], w[0]))):
                        nc.tensor.matmul(sums[:, 0, :], left, right, start=(part == 0), stop=False)
                elif step == "pairsT":
                    pe.wait_ge(packed_by_dve, n + 1)
                    pe.wait_ge(packed_by_act, n + 1)
                    if n == 0:
                        pe.wait_ge(packed_set, 2)
                    else:
                        pe.wait_ge(h1_low, PIECES * n)
                        pe.wait_ge(h2_biased, n)
                    for p in range(PIECES):
                        for at, c in enumerate(piece(p, PAIR_CHUNKS)):
                            last = nc.tensor.transpose(pairsT_piece(p)[:, P * at:P * (at + 1)],
                                                       packed[:, n % 2, P * c:P * (c + 1)], identity[:])
                        last.then_inc(pairs_turned, 1)
                elif step == "layer1":
                    if n == 0:
                        pe.wait_ge(load_low, SELECTED_COUNT + 2)
                    passes(sums[:, 0, :], n, PAIR_CHUNKS, pairs_h, pairs_l, w1_h, w1_l, pairs_high, pairs_low,
                           first=False).then_inc(h1_summed, 1)
                elif step == "hiddenT":
                    for p in range(PIECES):
                        pe.wait_ge(h1_done, PIECES * n + p + 1)
                        for at, c in enumerate(piece(p, N1)):
                            last = nc.tensor.transpose(hiddenT_piece(p)[:, P * at:P * (at + 1)],
                                                       h1[:, P * c:P * (c + 1)], identity[:])
                        last.then_inc(h1_turned, 1)
                elif step == "layer2":
                    if n == 0:
                        pe.wait_ge(load_low, LOADS)
                    else:
                        pe.wait_ge(h2_biased, n)
                    passes(sums[:, 1, 0:HIDDEN2], n, N1, h1T_h, h1T_l, w2_h, w2_l, h1_high, h1_low
                           ).then_inc(h2_summed, 1)


def pair_row(a, b):
    return a * (FEATURES - 1) - a * (a - 1) // 2 + (b - a - 1)


def arrange_w1(w, b):
    arranged = np.zeros((CHUNKS1 * P, HIDDEN1), w.dtype)
    for j in range(1, FEATURES):
        for i in range(j):
            arranged[packed_at(j) + i] = w[pair_row(*sorted((SLOT_FEATURE[i], SLOT_FEATURE[j])))]
    arranged[BIAS_AT] = b
    arranged[DENSE_CHUNK * P:] = w[FEATURES * (FEATURES - 1) // 2:]
    return arranged.reshape(CHUNKS1, P, HIDDEN1).transpose(1, 0, 2).reshape(P, CHUNKS1 * HIDDEN1)


def kernel(**inputs):
    import concourse.bacc as bacc
    from concourse.bass_utils import run_bass_kernel_spmd

    ids, dense = np.asarray(inputs["ids"]), np.asarray(inputs["r_dense"])
    w2 = np.asarray(inputs["W_top2"])
    host = {
        "idx": ids.reshape(TILES, P, TABLES).transpose(1, 0, 2).reshape(P, TILES * TABLES),
        "ids_by_table": ids.T[SELECTED],
        "dense_t": dense.T,
        **{f"tbl_{f}": np.asarray(inputs[f"tbl_{f}"]) for f in range(TABLES)},
        "w1": arrange_w1(np.asarray(inputs["W_top1"]), np.asarray(inputs["b_top1"])),
        "w2": w2.reshape(N1, P, HIDDEN2).transpose(1, 0, 2).reshape(P, N1 * HIDDEN2),
        "b2": np.asarray(inputs["b_top2"]).reshape(1, HIDDEN2),
        "w3": np.asarray(inputs["W_top3"]).reshape(1, HIDDEN2),
    }
    host = {name: np.ascontiguousarray(a) for name, a in host.items()}
    nc = bacc.Bacc("TRN2", target_bir_lowering=False, num_devices=1)
    aps = {name: nc.dram_tensor(name, a.shape, mybir.dt.from_np(a.dtype), kind="ExternalInput").ap()
           for name, a in host.items()}
    out = nc.dram_tensor("y_out", (B, 1), mybir.dt.float32, kind="ExternalOutput").ap()
    build(nc, aps["idx"], aps["ids_by_table"], aps["dense_t"], [aps[f"tbl_{f}"] for f in range(TABLES)],
          aps["w1"], aps["w2"], aps["b2"], aps["w3"], out)
    return run_bass_kernel_spmd(nc, [host], core_ids=[0]).results[0]["y_out"]
```
